# Optimizing a Trainium2 kernel written in Bass

```python
import numpy as np
import jax
import jax.numpy as jnp

def _softmax(x, axis=-1):
    return jax.nn.softmax(x, axis=axis)

def _gelu(x):
    return jax.nn.gelu(x, approximate=True)

def _silu(x):
    return jax.nn.silu(x)

def _sigmoid(x):
    return jax.nn.sigmoid(x)

def _layernorm(x, axis=-1, eps=1e-05):
    m = jnp.mean(x, axis=axis, keepdims=True)
    v = jnp.var(x, axis=axis, keepdims=True)
    return (x - m) / jnp.sqrt(v + eps)

def _scatter_add(tgt, idx, src, axis=0):
    return tgt.at[idx].add(src)

def _segment_sum(src, seg, n):
    return jax.ops.segment_sum(src, seg, n)
kernel_name = 'mk_dlrm_tower_d1_rec_r8_99a7f1'

def setup_inputs(seed: int=0):
    np.random.seed(seed)
    _w = jnp.asarray

    def _rec_inputs():
        import jax
        import jax.numpy as jnp
        _tk = jax.random.key(seed)
        dense_ctx = jax.random.normal(jax.random.fold_in(_tk, 190), (512, 16), jnp.float32)
        ids = jnp.stack([jax.random.randint(jax.random.fold_in(_tk, 200 + f), (512,), 0, v, jnp.int32) for f, v in enumerate([12500, 1000, 1000, 12500, 1000, 1000, 1000, 1250, 1000, 1250, 1000, 12500, 1250, 1250, 1000, 1250, 12500, 1000, 1250, 12500, 1000, 12500, 1250, 1250, 1000, 1250, 1250, 1000, 1000, 1000, 1000, 12500])], axis=1)
        tbl_0 = 0.05 * jax.random.normal(jax.random.fold_in(_tk, 500 + 0), (12500, 256), jnp.float32)
        tbl_1 = 0.05 * jax.random.normal(jax.random.fold_in(_tk, 500 + 1), (1000, 256), jnp.float32)
        tbl_2 = 0.05 * jax.random.normal(jax.random.fold_in(_tk, 500 + 2), (1000, 256), jnp.float32)
        tbl_3 = 0.05 * jax.random.normal(jax.random.fold_in(_tk, 500 + 3), (12500, 256), jnp.float32)
        tbl_4 = 0.05 * jax.random.normal(jax.random.fold_in(_tk, 500 + 4), (1000, 256), jnp.float32)
        tbl_5 = 0.05 * jax.random.normal(jax.random.fold_in(_tk, 500 + 5), (1000, 256), jnp.float32)
        tbl_6 = 0.05 * jax.random.normal(jax.random.fold_in(_tk, 500 + 6), (1000, 256), jnp.float32)
        tbl_7 = 0.05 * jax.random.normal(jax.random.fold_in(_tk, 500 + 7), (1250, 256), jnp.float32)
        tbl_8 = 0.05 * jax.random.normal(jax.random.fold_in(_tk, 500 + 8), (1000, 256), jnp.float32)
        tbl_9 = 0.05 * jax.random.normal(jax.random.fold_in(_tk, 500 + 9), (1250, 256), jnp.float32)
        tbl_10 = 0.05 * jax.random.normal(jax.random.fold_in(_tk, 500 + 10), (1000, 256), jnp.float32)
        tbl_11 = 0.05 * jax.random.normal(jax.random.fold_in(_tk, 500 + 11), (12500, 256), jnp.float32)
        tbl_12 = 0.05 * jax.random.normal(jax.random.fold_in(_tk, 500 + 12), (1250, 256), jnp.float32)
        tbl_13 = 0.05 * jax.random.normal(jax.random.fold_in(_tk, 500 + 13), (1250, 256), jnp.float32)
        tbl_14 = 0.05 * jax.random.normal(jax.random.fold_in(_tk, 500 + 14), (1000, 256), jnp.float32)
        tbl_15 = 0.05 * jax.random.normal(jax.random.fold_in(_tk, 500 + 15), (1250, 256), jnp.float32)
        tbl_16 = 0.05 * jax.random.normal(jax.random.fold_in(_tk, 500 + 16), (12500, 256), jnp.float32)
        tbl_17 = 0.05 * jax.random.normal(jax.random.fold_in(_tk, 500 + 17), (1000, 256), jnp.float32)
        tbl_18 = 0.05 * jax.random.normal(jax.random.fold_in(_tk, 500 + 18), (1250, 256), jnp.float32)
        tbl_19 = 0.05 * jax.random.normal(jax.random.fold_in(_tk, 500 + 19), (12500, 256), jnp.float32)
        tbl_20 = 0.05 * jax.random.normal(jax.random.fold_in(_tk, 500 + 20), (1000, 256), jnp.float32)
        tbl_21 = 0.05 * jax.random.normal(jax.random.fold_in(_tk, 500 + 21), (12500, 256), jnp.float32)
        tbl_22 = 0.05 * jax.random.normal(jax.random.fold_in(_tk, 500 + 22), (1250, 256), jnp.float32)
        tbl_23 = 0.05 * jax.random.normal(jax.random.fold_in(_tk, 500 + 23), (1250, 256), jnp.float32)
        tbl_24 = 0.05 * jax.random.normal(jax.random.fold_in(_tk, 500 + 24), (1000, 256), jnp.float32)
        tbl_25 = 0.05 * jax.random.normal(jax.random.fold_in(_tk, 500 + 25), (1250, 256), jnp.float32)
        tbl_26 = 0.05 * jax.random.normal(jax.random.fold_in(_tk, 500 + 26), (1250, 256), jnp.float32)
        tbl_27 = 0.05 * jax.random.normal(jax.random.fold_in(_tk, 500 + 27), (1000, 256), jnp.float32)
        tbl_28 = 0.05 * jax.random.normal(jax.random.fold_in(_tk, 500 + 28), (1000, 256), jnp.float32)
        tbl_29 = 0.05 * jax.random.normal(jax.random.fold_in(_tk, 500 + 29), (1000, 256), jnp.float32)
        tbl_30 = 0.05 * jax.random.normal(jax.random.fold_in(_tk, 500 + 30), (1000, 256), jnp.float32)
        tbl_31 = 0.05 * jax.random.normal(jax.random.fold_in(_tk, 500 + 31), (12500, 256), jnp.float32)
        _rk = jax.random.fold_in(_tk, 7)
        W_top1 = 0.0441942 * jax.random.normal(jax.random.fold_in(_tk, 801), (512, 512), jnp.float32)
        W_top2 = 0.0441942 * jax.random.normal(jax.random.fold_in(_tk, 802), (512, 256), jnp.float32)
        W_top3 = 0.0625 * jax.random.normal(jax.random.fold_in(_tk, 803), (256, 1), jnp.float32)
        b_top1 = jnp.zeros((512,), jnp.float32)
        b_top2 = jnp.zeros((256,), jnp.float32)
        return (dense_ctx, ids, tbl_0, tbl_1, tbl_2, tbl_3, tbl_4, tbl_5, tbl_6, tbl_7, tbl_8, tbl_9, tbl_10, tbl_11, tbl_12, tbl_13, tbl_14, tbl_15, tbl_16, tbl_17, tbl_18, tbl_19, tbl_20, tbl_21, tbl_22, tbl_23, tbl_24, tbl_25, tbl_26, tbl_27, tbl_28, tbl_29, tbl_30, tbl_31, W_top1, b_top1, W_top2, b_top2, W_top3)
    dense_ctx, ids, tbl_0, tbl_1, tbl_2, tbl_3, tbl_4, tbl_5, tbl_6, tbl_7, tbl_8, tbl_9, tbl_10, tbl_11, tbl_12, tbl_13, tbl_14, tbl_15, tbl_16, tbl_17, tbl_18, tbl_19, tbl_20, tbl_21, tbl_22, tbl_23, tbl_24, tbl_25, tbl_26, tbl_27, tbl_28, tbl_29, tbl_30, tbl_31, W_top1, b_top1, W_top2, b_top2, W_top3 = _rec_inputs()

    def _L0_rec_setup():
        import jax, jax.numpy as jnp
        import numpy as np
        B, N, D = (1024, 32, 256)
        key = jax.random.key(seed)
        x = jax.random.normal(key, (B, N, D), dtype=jnp.float32)
        return {'x': x}
    _L0_rec_all = _L0_rec_setup()
    _L0_rec_in = {k: v for k, v in _L0_rec_all.items() if k in ()}
    del _L0_rec_all
    return {'dense_ctx': dense_ctx, 'ids': ids, 'tbl_0': tbl_0, 'tbl_1': tbl_1, 'tbl_2': tbl_2, 'tbl_3': tbl_3, 'tbl_4': tbl_4, 'tbl_5': tbl_5, 'tbl_6': tbl_6, 'tbl_7': tbl_7, 'tbl_8': tbl_8, 'tbl_9': tbl_9, 'tbl_10': tbl_10, 'tbl_11': tbl_11, 'tbl_12': tbl_12, 'tbl_13': tbl_13, 'tbl_14': tbl_14, 'tbl_15': tbl_15, 'tbl_16': tbl_16, 'tbl_17': tbl_17, 'tbl_18': tbl_18, 'tbl_19': tbl_19, 'tbl_20': tbl_20, 'tbl_21': tbl_21, 'tbl_22': tbl_22, 'tbl_23': tbl_23, 'tbl_24': tbl_24, 'tbl_25': tbl_25, 'tbl_26': tbl_26, 'tbl_27': tbl_27, 'tbl_28': tbl_28, 'tbl_29': tbl_29, 'tbl_30': tbl_30, 'tbl_31': tbl_31, 'W_top1': W_top1, 'b_top1': b_top1, 'W_top2': W_top2, 'b_top2': b_top2, 'W_top3': W_top3}

def reference(dense_ctx, ids, tbl_0, tbl_1, tbl_2, tbl_3, tbl_4, tbl_5, tbl_6, tbl_7, tbl_8, tbl_9, tbl_10, tbl_11, tbl_12, tbl_13, tbl_14, tbl_15, tbl_16, tbl_17, tbl_18, tbl_19, tbl_20, tbl_21, tbl_22, tbl_23, tbl_24, tbl_25, tbl_26, tbl_27, tbl_28, tbl_29, tbl_30, tbl_31, W_top1, b_top1, W_top2, b_top2, W_top3):
    import jax
    import jax.numpy as jnp

    def _L0_rec_ref(x):
        import jax, jax.numpy as jnp
        import numpy as np
        B, N, D = (1024, 32, 256)
        'Second-order feature interaction (DLRM dot interaction).\n\n            Computes dot(x_i, x_j) for all field pairs i < j (self_interaction=False),\n            flattened in row-major upper-triangular order -> [B, N*(N-1)/2].\n            Matches tf.boolean_mask(dot_products, strictly_upper_mask) ordering.\n            '
        b, n, d = x.shape
        iu, ju = jnp.triu_indices(n, k=1)
        dots = jnp.einsum('bnd,bmd->bnm', x, x)
        return dots[:, iu, ju]
    e = jnp.stack([tbl_0[ids[:, 0]], tbl_1[ids[:, 1]], tbl_2[ids[:, 2]], tbl_3[ids[:, 3]], tbl_4[ids[:, 4]], tbl_5[ids[:, 5]], tbl_6[ids[:, 6]], tbl_7[ids[:, 7]], tbl_8[ids[:, 8]], tbl_9[ids[:, 9]], tbl_10[ids[:, 10]], tbl_11[ids[:, 11]], tbl_12[ids[:, 12]], tbl_13[ids[:, 13]], tbl_14[ids[:, 14]], tbl_15[ids[:, 15]], tbl_16[ids[:, 16]], tbl_17[ids[:, 17]], tbl_18[ids[:, 18]], tbl_19[ids[:, 19]], tbl_20[ids[:, 20]], tbl_21[ids[:, 21]], tbl_22[ids[:, 22]], tbl_23[ids[:, 23]], tbl_24[ids[:, 24]], tbl_25[ids[:, 25]], tbl_26[ids[:, 26]], tbl_27[ids[:, 27]], tbl_28[ids[:, 28]], tbl_29[ids[:, 29]], tbl_30[ids[:, 30]], tbl_31[ids[:, 31]]], axis=1)
    z = _L0_rec_ref(e)
    z = z.reshape(z.shape[0], -1)
    h = jnp.concatenate([z, dense_ctx], axis=1)
    h = jnp.maximum(h @ W_top1 + b_top1, 0.0)
    h = jnp.maximum(h @ W_top2 + b_top2, 0.0)
    y = h @ W_top3
    return y

_drawn_inputs = setup_inputs


def setup_inputs(seed=0):
    import zlib

    import numpy as np

    out = dict(_drawn_inputs(seed))
    spreads = {'b_top1': (0.0, 0.1), 'b_top2': (0.0, 0.1)}
    factors = {}
    for name, (base, spread) in spreads.items():
        noise = np.random.default_rng([zlib.crc32(name.encode()), seed]).standard_normal(out[name].shape)
        drawn = base * np.exp(spread * noise) if base else spread * noise
        out[name] = jnp.asarray(drawn.astype(out[name].dtype))
    for name, factor in factors.items():
        out[name] = (out[name] * factor).astype(out[name].dtype)
    return out
```

```python
from contextlib import ExitStack

import numpy as np

import concourse.bass as bass
from concourse import mybir
from concourse.alu_op_type import AluOpType as ALU

F32 = mybir.dt.float32
I32 = mybir.dt.int32

P = 128
FIELDS = 32
PER_GROUP = P // FIELDS
COLS = 8
QUADS = FIELDS // COLS
TILE_GROUPS = 16
TILE_PAIRS = TILE_GROUPS // 2
BATCH_GROUPS = 8
BATCH_PAIRS = BATCH_GROUPS // 2
BATCHES = TILE_GROUPS // BATCH_GROUPS
HALF = TILE_GROUPS // 2
TILE = TILE_GROUPS * PER_GROUP
XT_SLOTS = 4


def build(nc, tables, ids, table_base, w1_pairs, w1_dense, dense, w2, b2, w3, y):
    dim = tables.shape[1]
    halves = dim // P
    samples = dense.shape[1]
    dense_rows = dense.shape[0]
    n_groups = samples // PER_GROUP
    n_tiles = samples // TILE
    hid1 = w1_dense.shape[1]
    hid2 = w2.shape[1] // (hid1 // P)
    n1 = hid1 // P
    n2 = hid2 // P
    pair_cols = 2 * halves * P

    with ExitStack() as ctx:
        def sb(name, shape, dt=F32):
            return ctx.enter_context(nc.sbuf_tensor(name, shape, dt))

        def ps(name, shape):
            return ctx.enter_context(nc.psum_tensor(name, shape, F32))

        def sem(name):
            return ctx.enter_context(nc.semaphore(name))

        ids_sb = sb("ids_sb", [P, n_groups], I32)
        base_sb = sb("base_sb", [P, n_groups], I32)
        all_rows = sb("all_rows", [P, n_groups], I32)
        tile_rows = sb("tile_rows", [P, TILE_GROUPS], I32)
        ident = sb("ident", [P, P])
        x = sb("x", [P, TILE_GROUPS, dim])
        xt = sb("xt", [P, XT_SLOTS, 2, halves, P])
        z = sb("z", [P, COLS, TILE])
        w1p = sb("w1p", [P, COLS, hid1])
        w1d = sb("w1d", [dense_rows, hid1])
        dns = sb("dns", [dense_rows, samples])
        w2_sb = sb("w2_sb", [P, n1, hid2])
        b2_sb = sb("b2_sb", [P, n2])
        w3_sb = sb("w3_sb", [P, n2])
        h1 = sb("h1", [P, n1, TILE])
        h2 = sb("h2", [P, n2, TILE])
        y_row = sb("y_row", [1, samples])

        xt_ps = [ps(f"xt_ps{i}", [P, 2, halves, P]) for i in range(2)]
        dots_ps = [ps(f"dots_ps{i}", [P, BATCH_GROUPS, P]) for i in range(2)]
        h1_ps = ps("h1_ps", [P, n1, P])
        h2_ps = ps("h2_ps", [P, 4, P])

        ids_loaded = sem("ids_loaded")
        weights_loaded = sem("weights_loaded")
        all_rows_ready = sem("all_rows_ready")
        tile_rows_ready = sem("tile_rows_ready")
        ident_zeroed = sem("ident_zeroed")
        ident_ready = sem("ident_ready")
        gathered = [sem(f"gathered{i}") for i in range(TILE_PAIRS)]
        turned = sem("turned")
        xt_ready = sem("xt_ready")
        dots_done = sem("dots_done")
        z_ready = sem("z_ready")
        l1_done = sem("l1_done")
        h1_ready = sem("h1_ready")
        l2_done = sem("l2_done")
        h2_ready = sem("h2_ready")
        l3_done = sem("l3_done")
        y_ready = sem("y_ready")
        y_stored = sem("y_stored")

        block = ctx.enter_context(nc.Block())

        @block.sync
        def _(sp):
            sp.dma_start(ids_sb[:, :], ids).then_inc(ids_loaded, 16)
            sp.dma_start(base_sb[:, :], table_base).then_inc(ids_loaded, 16)
            sp.dma_start(w1p[:, :, :], w1_pairs.rearrange("p (c n) -> p c n", c=COLS)).then_inc(weights_loaded, 16)
            sp.dma_start(w1d[:, :], w1_dense).then_inc(weights_loaded, 16)
            sp.dma_start(dns[:, :], dense).then_inc(weights_loaded, 16)
            sp.dma_start(w2_sb[:, :, :], w2.rearrange("p (c n) -> p c n", c=n1)).then_inc(weights_loaded, 16)
            sp.dma_start(b2_sb[:, :], b2).then_inc(weights_loaded, 16)
            sp.dma_start(w3_sb[:, :], w3).then_inc(weights_loaded, 16)
            sp.wait_ge(y_ready, n_tiles)
            sp.dma_start(y, y_row[:, :]).then_inc(y_stored, 16)
            sp.wait_ge(y_stored, 16)

        weight_dmas = 6

        @block.gpsimd
        def _(pool):
            nc.gpsimd.memset(ident[:, :], 0.0).then_inc(ident_zeroed, 1)
            pool.wait_ge(ident_zeroed, 1)
            nc.gpsimd.affine_select(out=ident[:, :], in_=ident[:, :], compare_op=ALU.not_equal, fill=1.0,
                                    base=0, pattern=[[-1, P]], channel_multiplier=1).then_inc(ident_ready, 1)

            def gather_tile(t, first):
                for k in range(TILE_GROUPS):
                    if not first and k % 2 == 0:
                        pool.wait_ge(turned, (t - 1) * TILE_PAIRS + k // 2 + 1)
                        pool.nop(nofuse=True)
                    if k % HALF == 0:
                        pool.wait_ge(tile_rows_ready, t * 2 + k // HALF + 1)
                        pool.nop(nofuse=True)
                    nc.gpsimd.indirect_dma_start(
                        x[:, k, :], None, tables,
                        bass.IndirectOffsetOnAxis(tile_rows[:, k:k + 1], 0)).then_inc(gathered[k // 2], 16)

            gather_tile(0, True)
            with pool.Fori(1, n_tiles) as t:
                gather_tile(t, False)

        @block.tensor
        def _(pe):
            def turn(t, p, first):
                pe.wait_ge(gathered[p], (t + 1) * 32)
                if not (first and p < 2):
                    pe.wait_ge(xt_ready, t * TILE_PAIRS + p - 1)
                for q in range(2):
                    for h in range(halves):
                        last = nc.tensor.transpose(xt_ps[p % 2][:, q, h, :],
                                                   x[:, 2 * p + q, h * P:(h + 1) * P], ident[:, :])
                last.then_inc(turned, 1)

            def dots(t, p, first):
                pe.wait_ge(xt_ready, t * TILE_PAIRS + p + 1)
                b = p // BATCH_PAIRS
                if p % BATCH_PAIRS == 0 and not first:
                    pe.wait_ge(z_ready, (t - 1) * BATCHES + b + 1)
                for q in range(2):
                    for h in range(halves):
                        rows = xt[:, p % XT_SLOTS, q, h, :]
                        last = nc.tensor.matmul(dots_ps[b][:, 2 * (p % BATCH_PAIRS) + q, :], rows, rows,
                                                start=(h == 0), stop=(h == halves - 1))
                last.then_inc(dots_done, 1)

            def layer1(t, chunks, first):
                if 0 in chunks:
                    pe.wait_ge(z_ready, (t + 1) * BATCHES)
                    if not first:
                        pe.wait_ge(h1_ready, t)
                for n in chunks:
                    cols = slice(n * P, (n + 1) * P)
                    nc.tensor.matmul(h1_ps[:, n, 0:TILE], w1d[:, cols], dns[:, bass.ds(t * TILE, TILE)],
                                     start=True, stop=False)
                    for c in range(COLS):
                        last = nc.tensor.matmul(h1_ps[:, n, 0:TILE], w1p[:, c, cols], z[:, c, :],
                                                start=False, stop=(c == COLS - 1))
                    if n == n1 - 1:
                        last.then_inc(l1_done, 1)

            def layer2(t, first):
                pe.wait_ge(h1_ready, t + 1)
                if not first:
                    pe.wait_ge(y_ready, t)
                for n in range(n2):
                    for c in range(n1):
                        last = nc.tensor.matmul(h2_ps[:, n, 0:TILE], w2_sb[:, c, n * P:(n + 1) * P], h1[:, c, :],
                                                start=(c == 0), stop=(c == n1 - 1))
                last.then_inc(l2_done, 1)

            def layer3(t):
                pe.wait_ge(h2_ready, t + 1)
                for c in range(n2):
                    last = nc.tensor.matmul(h2_ps[0:1, n2, 0:TILE], w3_sb[:, c:c + 1], h2[:, c, :],
                                            start=(c == 0), stop=(c == n2 - 1))
                last.then_inc(l3_done, 1)

            def tile(t, first, second):
                for p in range(TILE_PAIRS):
                    turn(t, p, first)
                    if p > 0:
                        dots(t, p - 1, first)
                    elif not first:
                        dots(t - 1, TILE_PAIRS - 1, second)
                    if not first:
                        if p == 2:
                            layer1(t - 1, (0, 1), second)
                        if p == 3:
                            layer1(t - 1, (2, 3), second)
                        if p == 5:
                            layer2(t - 1, second)
                        if p == 7:
                            layer3(t - 1)

            pe.wait_ge(ident_ready, 1)
            tile(0, True, False)
            pe.wait_ge(weights_loaded, 16 * weight_dmas)
            tile(1, False, True)
            with pe.Fori(2, n_tiles) as t:
                tile(t, False, False)
            dots(n_tiles - 1, TILE_PAIRS - 1, False)
            layer1(n_tiles - 1, range(n1), False)
            layer2(n_tiles - 1, False)
            layer3(n_tiles - 1)

        @block.scalar
        def _(act):
            def next_rows(t, half):
                nc.scalar.copy(tile_rows[:, half * HALF:(half + 1) * HALF],
                               all_rows[:, bass.ds(t * TILE_GROUPS + half * HALF, HALF)]).then_inc(tile_rows_ready, 1)

            def tile(t, first, last):
                for p in range(TILE_PAIRS):
                    act.wait_ge(turned, t * TILE_PAIRS + p + 1)
                    if not (first and p < XT_SLOTS):
                        act.wait_ge(dots_done, t * TILE_PAIRS + p + 1 - XT_SLOTS)
                    nc.scalar.copy(xt[:, p % XT_SLOTS, :, :, :], xt_ps[p % 2][:, :, :, :]).then_inc(xt_ready, 1)
                    if (p + 1) % (TILE_PAIRS // 2) == 0 and not last:
                        if first and p < TILE_PAIRS // 2:
                            act.wait_ge(all_rows_ready, 1)
                        next_rows(t + 1, p // (TILE_PAIRS // 2))

            tile(0, True, False)
            with act.Fori(1, n_tiles - 1) as t:
                tile(t, False, False)
            tile(n_tiles - 1, False, True)

        @block.vector
        def _(dve):
            def lay_out(t, b, first):
                dve.wait_ge(dots_done, t * TILE_PAIRS + (b + 1) * BATCH_PAIRS)
                if b == 0 and not first:
                    dve.wait_ge(l1_done, t)
                zb = z[:, :, b * BATCH_GROUPS * PER_GROUP:(b + 1) * BATCH_GROUPS * PER_GROUP].rearrange(
                    "p c (g s) -> p s g c", s=PER_GROUP)
                for s in range(PER_GROUP):
                    for q in range(QUADS):
                        src = dots_ps[b][s * FIELDS:(s + 1) * FIELDS, :,
                                         s * FIELDS + q * COLS:s * FIELDS + (q + 1) * COLS]
                        last = nc.vector.tensor_copy(zb[q * FIELDS:(q + 1) * FIELDS, s, :, :], src)
                last.then_inc(z_ready, 1)

            def relu1(t, first):
                dve.wait_ge(l1_done, t + 1)
                if not first:
                    dve.wait_ge(l2_done, t)
                nc.vector.tensor_scalar(h1[:, :, :], h1_ps[:, :, 0:TILE], 0.0, None, ALU.max).then_inc(h1_ready, 1)

            def relu2(t, first):
                dve.wait_ge(l2_done, t + 1)
                if not first:
                    dve.wait_ge(l3_done, t)
                for n in range(n2):
                    last = nc.vector.tensor_scalar(h2[:, n, :], h2_ps[:, n, 0:TILE], b2_sb[:, n:n + 1], 0.0,
                                                   ALU.add, ALU.max)
                last.then_inc(h2_ready, 1)

            def store_y(t):
                dve.wait_ge(l3_done, t + 1)
                nc.vector.tensor_copy(y_row[:, bass.ds(t * TILE, TILE)],
                                      h2_ps[0:1, n2, 0:TILE]).then_inc(y_ready, 1)

            def tile(t, first, second):
                if not first:
                    relu1(t - 1, second)
                lay_out(t, 0, first)
                if not first:
                    relu2(t - 1, second)
                    store_y(t - 1)
                lay_out(t, 1, first)

            dve.wait_ge(ids_loaded, 32)
            nc.vector.tensor_tensor(tile_rows[:, :], ids_sb[:, 0:TILE_GROUPS], base_sb[:, 0:TILE_GROUPS],
                                    ALU.add).then_inc(tile_rows_ready, 2)
            nc.vector.tensor_tensor(all_rows[:, :], ids_sb[:, :], base_sb[:, :], ALU.add).then_inc(all_rows_ready, 1)
            tile(0, True, False)
            dve.wait_ge(weights_loaded, 16 * weight_dmas)
            tile(1, False, True)
            with dve.Fori(2, n_tiles) as t:
                tile(t, False, False)
            relu1(n_tiles - 1, False)
            relu2(n_tiles - 1, False)
            store_y(n_tiles - 1)


def kernel(**inputs):
    import concourse.bacc as bacc
    from concourse.bass_utils import run_bass_kernel_spmd as run

    tables = [np.asarray(inputs[f"tbl_{f}"]) for f in range(FIELDS)]
    base = np.cumsum([0] + [t.shape[0] for t in tables[:-1]]).astype(np.int32)
    ids = np.asarray(inputs["ids"])
    samples = ids.shape[0]
    groups = samples // PER_GROUP

    w1 = np.asarray(inputs["W_top1"])
    n_pairs = FIELDS * (FIELDS - 1) // 2
    rows_i, rows_j = np.triu_indices(FIELDS, k=1)
    w1_pairs = np.zeros((QUADS, FIELDS, COLS, w1.shape[1]), w1.dtype)
    w1_pairs[rows_j // COLS, rows_i, rows_j % COLS] = w1[:n_pairs]

    w2 = np.asarray(inputs["W_top2"])
    arrays = {
        "tables": np.concatenate(tables, axis=0),
        "ids": np.ascontiguousarray(
            ids.reshape(groups, PER_GROUP, FIELDS).transpose(1, 2, 0).reshape(P, groups)),
        "table_base": np.ascontiguousarray(np.broadcast_to(np.tile(base, PER_GROUP)[:, None], (P, groups))),
        "w1_pairs": w1_pairs.reshape(P, -1),
        "w1_dense": np.concatenate([w1[n_pairs:], np.asarray(inputs["b_top1"])[None, :]], axis=0),
        "dense": np.concatenate([np.asarray(inputs["dense_ctx"]).T, np.ones((1, samples), np.float32)], axis=0),
        "w2": np.ascontiguousarray(
            w2.reshape(-1, P, w2.shape[1]).transpose(1, 0, 2).reshape(P, -1)),
        "b2": np.ascontiguousarray(np.asarray(inputs["b_top2"]).reshape(-1, P).T),
        "w3": np.ascontiguousarray(np.asarray(inputs["W_top3"]).reshape(-1, P).T),
    }
    nc = bacc.Bacc("TRN2", target_bir_lowering=False, num_devices=1)
    aps = {k: nc.dram_tensor(k, v.shape, mybir.dt.from_np(v.dtype), kind="ExternalInput").ap()
           for k, v in arrays.items()}
    y = nc.dram_tensor("y", (1, samples), F32, kind="ExternalOutput").ap()
    build(nc, **aps, y=y)
    r = run(nc, [arrays], core_ids=[0])
    return r.results[0]["y"].reshape(samples, 1)
```

```python
from contextlib import ExitStack

import numpy as np

import concourse.bass as bass
from concourse import mybir
from concourse.alu_op_type import AluOpType as ALU

F32 = mybir.dt.float32
I32 = mybir.dt.int32

P = 128
FIELDS = 32
PER_GROUP = P // FIELDS
COLS = 8
QUADS = FIELDS // COLS
TILE_GROUPS = 32
TILE_PAIRS = TILE_GROUPS // 2
TILE = TILE_GROUPS * PER_GROUP
HALF_GROUPS = TILE_GROUPS // 2
HALF = TILE // 2
BATCH_PAIRS = 2
BATCH_GROUPS = 2 * BATCH_PAIRS
BATCH = BATCH_GROUPS * PER_GROUP
BATCHES = TILE_GROUPS // BATCH_GROUPS
XT_SLOTS = 4

LAY_OUT_STEP = {2: (0,), 4: (1,), 6: (2,), 8: (3,), 13: (4, 5), 15: (6,)}
LAYER1_STEP = {9: 0, 10: 1, 11: 2, 12: 3}
LAYER2_STEP = 14
LAYER3_STEP = 15


def build(nc, tables, ids, table_base, w1_pairs, w1_dense, dense, w2, b2, w3, y):
    dim = tables.shape[1]
    halves = dim // P
    samples = dense.shape[1]
    dense_rows = dense.shape[0]
    n_groups = samples // PER_GROUP
    n_tiles = samples // TILE
    hid1 = w1_dense.shape[1]
    n1 = hid1 // P
    n2 = w2.shape[1] // n1 // P
    hid2 = n2 * P
    assert len(LAYER1_STEP) == n1 and hid1 == 4 * P

    with ExitStack() as ctx:
        def sb(name, shape, dt=F32):
            return ctx.enter_context(nc.sbuf_tensor(name, shape, dt))

        def ps(name, shape):
            return ctx.enter_context(nc.psum_tensor(name, shape, F32))

        def sem(name):
            return ctx.enter_context(nc.semaphore(name))

        ids_sb = sb("ids_sb", [P, n_groups], I32)
        base_sb = sb("base_sb", [P, n_groups], I32)
        all_rows = sb("all_rows", [P, n_groups + HALF_GROUPS], I32)
        tile_rows = sb("tile_rows", [P, TILE_GROUPS], I32)
        ident = sb("ident", [P, P])
        fold = sb("fold", [P, HALF])
        x = sb("x", [P, TILE_GROUPS, dim])
        xt = sb("xt", [P, XT_SLOTS, 2, halves, P])
        z = sb("z", [P, COLS, TILE])
        w1p = sb("w1p", [P, COLS, hid1])
        w1d = sb("w1d", [dense_rows, hid1])
        dns = sb("dns", [dense_rows, samples])
        w2_sb = sb("w2_sb", [P, n1, hid2])
        b2_sb = sb("b2_sb", [P, n2])
        w3_sb = sb("w3_sb", [P, n2])
        h1 = sb("h1", [P, n1, TILE])
        h2 = sb("h2", [P, n2, TILE])
        h1_parts = sb("h1_parts", [P, hid1])
        y_row = sb("y_row", [1, samples])

        xt_ps = [ps(f"xt_ps{i}", [P, 2, halves, P]) for i in range(2)]
        dots_ps = [ps(f"dots_ps{i}", [P, BATCH_GROUPS, P]) for i in range(4)]
        h1_ps = ps("h1_ps", [P, n1, TILE])
        h2_ps = ps("h2_ps", [P, n2 + 1, TILE])

        ids_loaded = sem("ids_loaded")
        weights_loaded = sem("weights_loaded")
        all_rows_ready = sem("all_rows_ready")
        tile_rows_ready = sem("tile_rows_ready")
        ident_zeroed = sem("ident_zeroed")
        ident_ready = sem("ident_ready")
        fold_ready = sem("fold_ready")
        gathered = [sem(f"gathered{i}") for i in range(TILE_PAIRS)]
        turned = sem("turned")
        xt_ready = sem("xt_ready")
        dots_done = sem("dots_done")
        z_by_dve = sem("z_by_dve")
        z_by_act = sem("z_by_act")
        l1_done = sem("l1_done")
        h1_ready = sem("h1_ready")
        l2_done = sem("l2_done")
        h2_ready = sem("h2_ready")
        l3_done = sem("l3_done")
        y_ready = sem("y_ready")
        parts_done = sem("parts_done")
        parts_ready = sem("parts_ready")
        y_stored = sem("y_stored")

        block = ctx.enter_context(nc.Block())

        def block_cols(t):
            if isinstance(t, int) and t == 0:
                return slice(HALF, TILE), slice(0, HALF)
            return slice(0, TILE), bass.ds(t * TILE - HALF, TILE)

        @block.sync
        def _(sp):
            sp.dma_start(ids_sb[:, :], ids).then_inc(ids_loaded, 16)
            sp.dma_start(w1p[:, :, :], w1_pairs.rearrange("p (c n) -> p c n", c=COLS)).then_inc(weights_loaded, 16)
            sp.dma_start(w1d[:, :], w1_dense).then_inc(weights_loaded, 16)
            sp.dma_start(dns[:, :], dense).then_inc(weights_loaded, 16)
            sp.dma_start(w2_sb[:, :, :], w2.rearrange("p (c n) -> p c n", c=n1)).then_inc(weights_loaded, 16)
            sp.dma_start(b2_sb[:, :], b2).then_inc(weights_loaded, 16)
            sp.dma_start(w3_sb[:, :], w3).then_inc(weights_loaded, 16)
            sp.wait_ge(y_ready, n_tiles + 1)
            sp.dma_start(y, y_row[:, :]).then_inc(y_stored, 16)
            sp.wait_ge(y_stored, 16)

        weight_dmas = 6

        @block.gpsimd
        def _(pool):
            nc.gpsimd.memset(ident[:, :], 0.0).then_inc(ident_zeroed, 1)
            pool.wait_ge(ident_zeroed, 1)
            nc.gpsimd.affine_select(out=ident[:, :], in_=ident[:, :], compare_op=ALU.not_equal, fill=1.0,
                                    base=0, pattern=[[-1, P]], channel_multiplier=1).then_inc(ident_ready, 1)

            def gather_tile(t, first):
                for k in range(TILE_GROUPS):
                    if not first and k % 2 == 0:
                        pool.wait_ge(turned, (t - 1) * TILE_PAIRS + k // 2 + 1)
                        pool.nop(nofuse=True)
                    if k % HALF_GROUPS == 0:
                        pool.wait_ge(tile_rows_ready, t * 2 + k // HALF_GROUPS + 1)
                        pool.nop(nofuse=True)
                    nc.gpsimd.indirect_dma_start(
                        x[:, k, :], None, tables,
                        bass.IndirectOffsetOnAxis(tile_rows[:, k:k + 1], 0)).then_inc(gathered[k // 2], 16)

            gather_tile(0, True)
            with pool.Fori(1, n_tiles) as t:
                gather_tile(t, False)

        @block.tensor
        def _(pe):
            def turn(t, p, first):
                pe.wait_ge(gathered[p], (t + 1) * 32)
                if not (first and p < 2):
                    pe.wait_ge(xt_ready, t * TILE_PAIRS + p - 1)
                for q in range(2):
                    for h in range(halves):
                        last = nc.tensor.transpose(xt_ps[p % 2][:, q, h, :],
                                                   x[:, 2 * p + q, h * P:(h + 1) * P], ident[:, :])
                last.then_inc(turned, 1)

            def dots(t, p, first):
                pe.wait_ge(xt_ready, t * TILE_PAIRS + p + 1)
                b = p // BATCH_PAIRS
                if p % BATCH_PAIRS == 0 and not (first and b < 4):
                    pe.wait_ge(z_by_dve, t * BATCHES + b - 3)
                    pe.wait_ge(z_by_act, t * BATCHES + b - 3)
                for q in range(2):
                    for h in range(halves):
                        rows = xt[:, p % XT_SLOTS, q, h, :]
                        last = nc.tensor.matmul(dots_ps[b % 4][:, 2 * (p % BATCH_PAIRS) + q, :], rows, rows,
                                                start=(h == 0), stop=(h == halves - 1))
                last.then_inc(dots_done, 1)

            def layer1(t, n, first):
                if n == 0:
                    pe.wait_ge(z_by_dve, t * BATCHES + BATCHES // 2)
                    pe.wait_ge(z_by_act, t * BATCHES + BATCHES // 2)
                    if first:
                        pe.wait_ge(weights_loaded, 16 * weight_dmas)
                    else:
                        pe.wait_ge(h1_ready, t)
                cols = slice(n * P, (n + 1) * P)
                zc, sc = block_cols(t)
                nc.tensor.matmul(h1_ps[:, n, zc], w1d[:, cols], dns[:, sc], start=True, stop=False)
                for c in range(COLS):
                    last = nc.tensor.matmul(h1_ps[:, n, zc], w1p[:, c, cols], z[:, c, zc],
                                            start=False, stop=(c == COLS - 1))
                if n == n1 - 1:
                    last.then_inc(l1_done, 1)

            def layer2(t, zc, first):
                pe.wait_ge(h1_ready, t + 1)
                if not first:
                    pe.wait_ge(y_ready, t)
                for n in range(n2):
                    for c in range(n1):
                        last = nc.tensor.matmul(h2_ps[:, n, zc], w2_sb[:, c, n * P:(n + 1) * P], h1[:, c, zc],
                                                start=(c == 0), stop=(c == n1 - 1))
                last.then_inc(l2_done, 1)

            def layer3(t, zc):
                pe.wait_ge(h2_ready, t + 1)
                for c in range(n2):
                    last = nc.tensor.matmul(h2_ps[0:1, n2, zc], w3_sb[:, c:c + 1], h2[:, c, zc],
                                            start=(c == 0), stop=(c == n2 - 1))
                last.then_inc(l3_done, 1)

            def tile(t, first):
                for p in range(TILE_PAIRS):
                    turn(t, p, first)
                    if p > 0:
                        dots(t, p - 1, first)
                    elif not first:
                        dots(t - 1, TILE_PAIRS - 1, False)
                    if p in LAYER1_STEP:
                        layer1(t, LAYER1_STEP[p], first)
                    if p == LAYER2_STEP:
                        layer2(t, block_cols(t)[0], first)
                    if p == LAYER3_STEP:
                        layer3(t, block_cols(t)[0])

            pe.wait_ge(ident_ready, 1)
            tile(0, True)
            with pe.Fori(1, n_tiles) as t:
                tile(t, False)

            dots(n_tiles - 1, TILE_PAIRS - 1, False)
            parts = h1_ps[:, :, :].rearrange("p n b -> p (n b)")
            last_cols = slice(0, HALF)
            pe.wait_ge(h1_ready, n_tiles)
            nc.tensor.matmul(parts[0:HALF, :], dns[:, samples - HALF:samples], w1d[:, :], start=True, stop=False)
            pe.wait_ge(z_by_dve, n_tiles * BATCHES)
            pe.wait_ge(z_by_act, n_tiles * BATCHES)
            for c in range(COLS):
                part = c % 2
                last = nc.tensor.matmul(parts[part * HALF:(part + 1) * HALF, :], z[:, c, last_cols], w1p[:, c, :],
                                        start=(c == 1), stop=(c >= COLS - 2))
            last.then_inc(parts_done, 1)
            pe.wait_ge(parts_ready, 1)
            pe.wait_ge(fold_ready, 1)
            for n in range(n1):
                last = nc.tensor.matmul(h1_ps[:, n, last_cols], h1_parts[:, n * P:(n + 1) * P], fold[:, :],
                                        start=True, stop=True)
            last.then_inc(l1_done, 1)
            layer2(n_tiles, last_cols, False)
            layer3(n_tiles, last_cols)

        def lay_out(engine_copy, b, share):
            start = (b * BATCH + HALF) % TILE
            zb = z[:, :, start:start + BATCH].rearrange("p c (g s) -> p s g c", s=PER_GROUP)
            for s in share:
                for q in range(QUADS):
                    src = dots_ps[b % 4][s * FIELDS:(s + 1) * FIELDS, :,
                                         s * FIELDS + q * COLS:s * FIELDS + (q + 1) * COLS]
                    last = engine_copy(zb[q * FIELDS:(q + 1) * FIELDS, s, :, :], src)
            return last

        @block.scalar
        def _(act):
            act.dma_start(base_sb[:, :], table_base).then_inc(ids_loaded, 16)

            def next_rows(t, half):
                nc.scalar.copy(tile_rows[:, half * HALF_GROUPS:(half + 1) * HALF_GROUPS],
                               all_rows[:, bass.ds(t * TILE_GROUPS + half * HALF_GROUPS, HALF_GROUPS)]
                               ).then_inc(tile_rows_ready, 1)

            def lay_out_batch(t, b):
                act.wait_ge(dots_done, t * TILE_PAIRS + (b + 1) * BATCH_PAIRS)
                if b == BATCHES // 2:
                    act.wait_ge(l1_done, t + 1)
                lay_out(nc.scalar.copy, b, range(PER_GROUP // 2, PER_GROUP)).then_inc(z_by_act, 1)

            def tile(t, first):
                for p in range(TILE_PAIRS):
                    act.wait_ge(turned, t * TILE_PAIRS + p + 1)
                    if not (first and p < XT_SLOTS):
                        act.wait_ge(dots_done, t * TILE_PAIRS + p + 1 - XT_SLOTS)
                    nc.scalar.copy(xt[:, p % XT_SLOTS, :, :, :], xt_ps[p % 2][:, :, :, :]).then_inc(xt_ready, 1)
                    if p == 0 and not first:
                        lay_out_batch(t - 1, BATCHES - 1)
                        next_rows(t, 1)
                    if p == TILE_PAIRS // 2:
                        next_rows(t + 1, 0)
                    for b in LAY_OUT_STEP.get(p, ()):
                        lay_out_batch(t, b)

            act.wait_ge(all_rows_ready, 2)
            tile(0, True)
            with act.Fori(1, n_tiles) as t:
                tile(t, False)
            lay_out_batch(n_tiles - 1, BATCHES - 1)

        @block.vector
        def _(dve):
            def lay_out_batch(t, b, first):
                dve.wait_ge(dots_done, t * TILE_PAIRS + (b + 1) * BATCH_PAIRS)
                if b == 0 and not first:
                    dve.wait_ge(l1_done, t)
                if b == BATCHES // 2:
                    dve.wait_ge(l1_done, t + 1)
                lay_out(nc.vector.tensor_copy, b, range(PER_GROUP // 2)).then_inc(z_by_dve, 1)

            def relu1(t, zc, first):
                dve.wait_ge(l1_done, t + 1)
                if not first:
                    dve.wait_ge(l2_done, t)
                nc.vector.tensor_scalar(h1[:, :, zc], h1_ps[:, :, zc], 0.0, None, ALU.max).then_inc(h1_ready, 1)

            def relu2(t, zc, first):
                dve.wait_ge(l2_done, t + 1)
                if not first:
                    dve.wait_ge(l3_done, t)
                for n in range(n2):
                    last = nc.vector.tensor_scalar(h2[:, n, zc], h2_ps[:, n, zc], b2_sb[:, n:n + 1], 0.0,
                                                   ALU.add, ALU.max)
                last.then_inc(h2_ready, 1)

            def store_y(t, zc, sc):
                dve.wait_ge(l3_done, t + 1)
                nc.vector.tensor_copy(y_row[:, sc], h2_ps[0:1, n2, zc]).then_inc(y_ready, 1)

            def tile(t, first):
                zc, sc = block_cols(t)
                for p in range(TILE_PAIRS):
                    if p == 0 and not first:
                        lay_out_batch(t - 1, BATCHES - 1, False)
                    if p - 1 == max(LAYER1_STEP):
                        relu1(t, zc, first)
                    if p - 1 == LAYER2_STEP:
                        relu2(t, zc, first)
                    for b in LAY_OUT_STEP.get(p, ()):
                        lay_out_batch(t, b, first)
                store_y(t, zc, sc)

            dve.wait_ge(ids_loaded, 32)
            nc.vector.tensor_tensor(tile_rows[:, :], ids_sb[:, 0:TILE_GROUPS], base_sb[:, 0:TILE_GROUPS],
                                    ALU.add).then_inc(tile_rows_ready, 2)
            nc.vector.tensor_tensor(all_rows[:, 0:n_groups], ids_sb[:, :], base_sb[:, :],
                                    ALU.add).then_inc(all_rows_ready, 1)
            nc.vector.memset(all_rows[:, n_groups:], 0).then_inc(all_rows_ready, 1)
            dve.wait_ge(ident_ready, 1)
            nc.vector.tensor_tensor(fold[:, :], ident[:, 0:HALF], ident[:, HALF:TILE], ALU.add).then_inc(fold_ready, 1)
            dve.wait_ge(weights_loaded, 16 * weight_dmas)
            tile(0, True)
            with dve.Fori(1, n_tiles) as t:
                tile(t, False)
            lay_out_batch(n_tiles - 1, BATCHES - 1, False)
            last_cols = slice(0, HALF)
            dve.wait_ge(parts_done, 1)
            nc.vector.tensor_copy(h1_parts[:, :], h1_ps[:, :, :].rearrange("p n b -> p (n b)")).then_inc(parts_ready, 1)
            relu1(n_tiles, last_cols, False)
            relu2(n_tiles, last_cols, False)
            store_y(n_tiles, last_cols, slice(samples - HALF, samples))


def kernel(**inputs):
    import concourse.bacc as bacc
    from concourse.bass_utils import run_bass_kernel_spmd as run

    tables = [np.asarray(inputs[f"tbl_{f}"]) for f in range(FIELDS)]
    base = np.cumsum([0] + [t.shape[0] for t in tables[:-1]]).astype(np.int32)
    ids = np.asarray(inputs["ids"])
    samples = ids.shape[0]
    groups = samples // PER_GROUP

    w1 = np.asarray(inputs["W_top1"])
    n_pairs = FIELDS * (FIELDS - 1) // 2
    rows_i, rows_j = np.triu_indices(FIELDS, k=1)
    w1_pairs = np.zeros((QUADS, FIELDS, COLS, w1.shape[1]), w1.dtype)
    w1_pairs[rows_j // COLS, rows_i, rows_j % COLS] = w1[:n_pairs]

    w2 = np.asarray(inputs["W_top2"])
    arrays = {
        "tables": np.concatenate(tables, axis=0),
        "ids": np.ascontiguousarray(
            ids.reshape(groups, PER_GROUP, FIELDS).transpose(1, 2, 0).reshape(P, groups)),
        "table_base": np.ascontiguousarray(np.broadcast_to(np.tile(base, PER_GROUP)[:, None], (P, groups))),
        "w1_pairs": w1_pairs.reshape(P, -1),
        "w1_dense": np.concatenate([w1[n_pairs:], np.asarray(inputs["b_top1"])[None, :]], axis=0),
        "dense": np.concatenate([np.asarray(inputs["dense_ctx"]).T, np.ones((1, samples), np.float32)], axis=0),
        "w2": np.ascontiguousarray(
            w2.reshape(-1, P, w2.shape[1]).transpose(1, 0, 2).reshape(P, -1)),
        "b2": np.ascontiguousarray(np.asarray(inputs["b_top2"]).reshape(-1, P).T),
        "w3": np.ascontiguousarray(np.asarray(inputs["W_top3"]).reshape(-1, P).T),
    }
    nc = bacc.Bacc("TRN2", target_bir_lowering=False, num_devices=1)
    aps = {k: nc.dram_tensor(k, v.shape, mybir.dt.from_np(v.dtype), kind="ExternalInput").ap()
           for k, v in arrays.items()}
    y = nc.dram_tensor("y", (1, samples), F32, kind="ExternalOutput").ap()
    build(nc, **aps, y=y)
    r = run(nc, [arrays], core_ids=[0])
    return r.results[0]["y"].reshape(samples, 1)
```

```python
from contextlib import ExitStack

import numpy as np

import concourse.bass as bass
from concourse import mybir
from concourse.alu_op_type import AluOpType as ALU

F32 = mybir.dt.float32
I32 = mybir.dt.int32

P = 128
FIELDS = 32
PER_GROUP = P // FIELDS
UPPER = FIELDS // 2
QUADS = P // FIELDS
COLS = UPPER // QUADS
DUO = 2 * FIELDS
TILE_GROUPS = 32
TILE_PAIRS = TILE_GROUPS // 2
TILE = TILE_GROUPS * PER_GROUP
HALF_GROUPS = TILE_GROUPS // 2
HALF = TILE // 2
BATCH_PAIRS = 2
BATCH_GROUPS = 2 * BATCH_PAIRS
BATCH = BATCH_GROUPS * PER_GROUP
BATCHES = TILE_GROUPS // BATCH_GROUPS
XT_SLOTS = 4

LAYER1_FROM = TILE_PAIRS // 2
LAYER1_UNITS = (4, 4, 3, 3, 3, 3)
LAYER2_FROM = LAYER1_FROM + len(LAYER1_UNITS)
LAYER3_STEP = 1


def build(nc, tables, ids, w1_slots, w1_dense, upper, dense, w2, b2, w3, y):
    dim = tables.shape[1]
    halves = dim // P
    samples = y.shape[1]
    dense_rows = dense.shape[0]
    n_groups = samples // PER_GROUP
    n_tiles = samples // TILE
    hid1 = w1_slots.shape[1] // COLS
    n1 = hid1 // P
    n2 = w2.shape[1] // n1 // P
    hid2 = n2 * P
    assert n1 * TILE == 512
    assert LAYER2_FROM + n2 == TILE_PAIRS

    with ExitStack() as ctx:
        def sb(name, shape, dt=F32):
            return ctx.enter_context(nc.sbuf_tensor(name, shape, dt))

        def ps(name, shape):
            return ctx.enter_context(nc.psum_tensor(name, shape, F32))

        def sem(name):
            return ctx.enter_context(nc.semaphore(name))

        ids_sb = sb("ids_sb", [P, 1 + n_groups], I32)
        all_rows = sb("all_rows", [P, n_groups], I32)
        tile_rows = sb("tile_rows", [P, TILE_GROUPS], I32)
        ident = sb("ident", [P, P])
        x = sb("x", [P, TILE_GROUPS, dim])
        xt = sb("xt", [P, XT_SLOTS, 2, halves, P])
        merged = [sb(f"merged{i}", [P, BATCH_GROUPS, 2, UPPER]) for i in range(2)]
        upper_sb = sb("upper_sb", [P, UPPER], I32)
        z = sb("z", [P, COLS, TILE])
        z_last = sb("z_last", [P, COLS, HALF])
        w1_sb = sb("w1_sb", [P, COLS, hid1])
        dense_sb = sb("dense_sb", [dense_rows, HALF + samples])
        w1_dense_sb = sb("w1_dense_sb", [dense_rows, hid1])
        w2_sb = sb("w2_sb", [P, n1, hid2])
        b2_sb = sb("b2_sb", [P, n2])
        w3_sb = sb("w3_sb", [P, n2])
        h1 = sb("h1", [P, n1, TILE])
        h2 = sb("h2", [P, n2, TILE])
        h1_last = sb("h1_last", [P, n1, HALF])
        h2_last = sb("h2_last", [P, n2, HALF])
        y_row = sb("y_row", [1, HALF + samples])

        xt_ps = [ps(f"xt_ps{i}", [P, 2, halves, P]) for i in range(2)]
        dots_ps = [ps(f"dots_ps{i}", [P, 2 * BATCH_GROUPS, DUO]) for i in range(4)]
        h1_ps = ps("h1_ps", [P, n1, TILE])
        h2_ps = ps("h2_ps", [P, n2 + 2, TILE])
        h1_last_ps = [h1_ps[:, 0, 0:HALF], xt_ps[0][:, 0, 0, 0:HALF], dots_ps[0][:, 0, :], dots_ps[1][:, 0, :]]
        h2_last_ps = [dots_ps[2][:, 0, :], dots_ps[3][:, 0, :]]
        assert (n1, n2) == (len(h1_last_ps), len(h2_last_ps))

        ids_loaded = sem("ids_loaded")
        upper_loaded = sem("upper_loaded")
        weights_loaded = sem("weights_loaded")
        z_cleared = sem("z_cleared")
        all_rows_ready = sem("all_rows_ready")
        tile_rows_ready = sem("tile_rows_ready")
        ident_zeroed = sem("ident_zeroed")
        ident_ready = sem("ident_ready")
        gathered = [sem(f"gathered{i}") for i in range(TILE_PAIRS)]
        turned = sem("turned")
        xt_ready = sem("xt_ready")
        dots_done = sem("dots_done")
        shuffled = sem("shuffled")
        merged_ready = sem("merged_ready")
        z_by_dve = sem("z_by_dve")
        z_by_act = sem("z_by_act")
        l1_done = sem("l1_done")
        h1_ready = sem("h1_ready")
        l2_done = sem("l2_done")
        h2_ready = sem("h2_ready")
        l3_done = sem("l3_done")
        y_ready = sem("y_ready")
        last_l1_done = sem("last_l1_done")
        last_h1_ready = sem("last_h1_ready")
        last_l2_done = sem("last_l2_done")
        last_h2_ready = sem("last_h2_ready")
        last_l3_done = sem("last_l3_done")
        y_stored = sem("y_stored")

        block = ctx.enter_context(nc.Block())

        @block.sync
        def _(sp):
            sp.dma_start(ids_sb[:, :], ids).then_inc(ids_loaded, 16)
            sp.dma_start(upper_sb[:, :], upper).then_inc(upper_loaded, 16)
            sp.dma_start(w1_sb[:, :, :], w1_slots.rearrange("p (c n) -> p c n", c=COLS)).then_inc(weights_loaded, 16)
            sp.dma_start(w1_dense_sb[:, :], w1_dense).then_inc(weights_loaded, 16)
            sp.dma_start(dense_sb[:, :], dense).then_inc(weights_loaded, 16)
            sp.dma_start(w2_sb[:, :, :], w2.rearrange("p (c n) -> p c n", c=n1)).then_inc(weights_loaded, 16)
            sp.dma_start(b2_sb[:, :], b2).then_inc(weights_loaded, 16)
            sp.dma_start(w3_sb[:, :], w3).then_inc(weights_loaded, 16)
            sp.wait_ge(y_ready, n_tiles + 1)
            sp.dma_start(y, y_row[:, HALF:]).then_inc(y_stored, 16)
            sp.wait_ge(y_stored, 16)

        weight_dmas = 6

        @block.gpsimd
        def _(pool):
            nc.gpsimd.memset(ident[:, :], 0.0).then_inc(ident_zeroed, 1)
            pool.wait_ge(ident_zeroed, 1)
            nc.gpsimd.affine_select(out=ident[:, :], in_=ident[:, :], compare_op=ALU.not_equal, fill=1.0,
                                    base=0, pattern=[[-1, P]], channel_multiplier=1).then_inc(ident_ready, 1)

            def gather_tile(t, first):
                for k in range(TILE_GROUPS):
                    if not first and k % 2 == 0:
                        pool.wait_ge(turned, (t - 1) * TILE_PAIRS + k // 2 + 1)
                        pool.nop(nofuse=True)
                    if k % HALF_GROUPS == 0:
                        pool.wait_ge(tile_rows_ready, t * 2 + k // HALF_GROUPS + 1)
                        pool.nop(nofuse=True)
                    nc.gpsimd.indirect_dma_start(
                        x[:, k, :], None, tables,
                        bass.IndirectOffsetOnAxis(tile_rows[:, k:k + 1], 0)).then_inc(gathered[k // 2], 16)

            gather_tile(0, True)
            with pool.Fori(1, n_tiles) as t:
                gather_tile(t, False)

        @block.tensor
        def _(pe):
            def turn(t, p, first):
                pe.wait_ge(gathered[p], (t + 1) * 32)
                if not (first and p < 2):
                    pe.wait_ge(xt_ready, t * TILE_PAIRS + p - 1)
                for q in range(2):
                    for h in range(halves):
                        last = nc.tensor.transpose(xt_ps[p % 2][:, q, h, :],
                                                   x[:, 2 * p + q, h * P:(h + 1) * P], ident[:, :])
                last.then_inc(turned, 1)

            def dots(t, p, first):
                pe.wait_ge(xt_ready, t * TILE_PAIRS + p + 1)
                b = p // BATCH_PAIRS
                if p % BATCH_PAIRS == 0 and not (first and b < 4):
                    pe.wait_ge(merged_ready, t * BATCHES + b - 3)
                for q in range(2):
                    for h in range(halves):
                        for u in range(2):
                            part = slice(u * DUO, (u + 1) * DUO)
                            rows = xt[:, p % XT_SLOTS, q, h, part]
                            last = nc.tensor.matmul(dots_ps[b % 4][part, 2 * (p % BATCH_PAIRS) + q, :], rows, rows,
                                                    start=(h == 0), stop=(h == halves - 1))
                last.then_inc(dots_done, 1)

            def layer1(t, first, units):
                for n, c in units:
                    outputs = slice(n * P, (n + 1) * P)
                    if c is None:
                        if n == 0 and first:
                            pe.wait_ge(weights_loaded, 16 * weight_dmas)
                        if n == 0 and not first:
                            pe.wait_ge(h1_ready, t)
                        nc.tensor.matmul(h1_ps[:, n, :], w1_dense_sb[:, outputs],
                                         dense_sb[:, bass.ds(t * TILE, TILE)], start=True, stop=False)
                        continue
                    if n == 0 and c == 0:
                        pe.wait_ge(z_by_dve, t * BATCHES + BATCHES // 2)
                        pe.wait_ge(z_by_act, t * BATCHES + BATCHES // 2)
                    last = nc.tensor.matmul(h1_ps[:, n, :], w1_sb[:, c, outputs], z[:, c, :],
                                            start=False, stop=(c == COLS - 1))
                    if (n, c) == (n1 - 1, COLS - 1):
                        last.then_inc(l1_done, 1)

            def layer2(t, first, n):
                if n == 0:
                    pe.wait_ge(h1_ready, t + 1)
                    if not first:
                        pe.wait_ge(y_ready, t)
                for c in range(n1):
                    last = nc.tensor.matmul(h2_ps[:, n, :], w2_sb[:, c, n * P:(n + 1) * P], h1[:, c, :],
                                            start=(c == 0), stop=(c == n1 - 1))
                if n == n2 - 1:
                    last.then_inc(l2_done, 1)

            def layer3(t):
                pe.wait_ge(h2_ready, t + 1)
                for c in range(n2):
                    last = nc.tensor.matmul(h2_ps[0:1, n2, :], w3_sb[:, c:c + 1], h2[:, c, :],
                                            start=(c == 0), stop=(c == n2 - 1))
                last.then_inc(l3_done, 1)

            layer1_units = [(n, c) for n in range(n1) for c in (None, *range(COLS))]
            assert sum(LAYER1_UNITS) == len(layer1_units)

            def tile(t, first):
                for p in range(TILE_PAIRS):
                    turn(t, p, first)
                    if LAYER1_FROM <= p < LAYER2_FROM:
                        k = p - LAYER1_FROM
                        layer1(t, first, layer1_units[sum(LAYER1_UNITS[:k]):sum(LAYER1_UNITS[:k + 1])])
                    if p >= LAYER2_FROM:
                        layer2(t, first, p - LAYER2_FROM)
                    if p == LAYER3_STEP and not first:
                        layer3(t - 1)
                    if 0 < p < LAYER1_FROM:
                        dots(t, p - 1, first)
                    if p >= LAYER1_FROM - 1:
                        dots(t, p, first)

            pe.wait_ge(ident_ready, 1)
            tile(0, True)
            with pe.Fori(1, n_tiles) as t:
                tile(t, False)
            layer3(n_tiles - 1)

            def last_matmul(out, weights, n, ins, start, stop):
                for u in range(2):
                    at = n * P + u * DUO
                    last = nc.tensor.matmul(out[u * DUO:(u + 1) * DUO], weights[:, at:at + DUO], ins,
                                            start=start, stop=stop)
                return last

            for n in range(n1):
                last_matmul(h1_last_ps[n], w1_dense_sb, n, dense_sb[:, samples:], True, False)
            pe.wait_ge(z_by_dve, n_tiles * BATCHES)
            pe.wait_ge(z_by_act, n_tiles * BATCHES)
            for n in range(n1):
                for c in range(COLS):
                    last = last_matmul(h1_last_ps[n], w1_sb[:, c, :], n, z_last[:, c, :], False, c == COLS - 1)
                last.then_inc(last_l1_done, 1)
            for i in range(2):
                pe.wait_ge(last_h1_ready, (i + 1) * n1 // 2)
                for n in range(n2):
                    for c in range(i * n1 // 2, (i + 1) * n1 // 2):
                        last = last_matmul(h2_last_ps[n], w2_sb[:, c, :], n, h1_last[:, c, :],
                                           c == 0, c == n1 - 1)
                    if i == 1:
                        last.then_inc(last_l2_done, 1)
            for c in range(n2):
                pe.wait_ge(last_h2_ready, c + 1)
                last = nc.tensor.matmul(h2_ps[0:1, n2 + 1, 0:HALF], w3_sb[:, c:c + 1], h2_last[:, c, :],
                                        start=(c == 0), stop=(c == n2 - 1))
            last.then_inc(last_l3_done, 1)

        def lay_out(engine_copy, b, in_last, share):
            start = (b * BATCH + HALF) % TILE
            to = z_last if in_last and b >= BATCHES // 2 else z
            zb = to[:, :, start:start + BATCH].rearrange("p c (g s) -> p s g c", s=PER_GROUP)
            for s in share:
                for q in range(QUADS):
                    last = engine_copy(zb[q * FIELDS:(q + 1) * FIELDS, s, :, :],
                                       merged[b % 2][s * FIELDS:(s + 1) * FIELDS, :, s % 2, q * COLS:(q + 1) * COLS])
            return last

        @block.scalar
        def _(act):
            def next_rows(t, half):
                nc.scalar.copy(tile_rows[:, half * HALF_GROUPS:(half + 1) * HALF_GROUPS],
                               all_rows[:, bass.ds(t * TILE_GROUPS + half * HALF_GROUPS, HALF_GROUPS)]
                               ).then_inc(tile_rows_ready, 1)

            def lay_out_batch(t, b, in_last):
                act.wait_ge(merged_ready, t * BATCHES + b + 1)
                if b == BATCHES // 2 and not in_last:
                    act.wait_ge(l1_done, t + 1)
                lay_out(nc.scalar.copy, b, in_last, range(PER_GROUP // 2, PER_GROUP)).then_inc(z_by_act, 1)

            def tile(t, first, in_last):
                for p in range(TILE_PAIRS):
                    act.wait_ge(turned, t * TILE_PAIRS + p + 1)
                    if not (first and p < XT_SLOTS):
                        act.wait_ge(dots_done, t * TILE_PAIRS + p + 1 - XT_SLOTS)
                    nc.scalar.copy(xt[:, p % XT_SLOTS, :, :, :], xt_ps[p % 2][:, :, :, :]).then_inc(xt_ready, 1)
                    if p == 0 and not first:
                        next_rows(t, 1)
                    if p == TILE_PAIRS // 2 and not in_last:
                        next_rows(t + 1, 0)
                    if BATCH_PAIRS < p < LAYER1_FROM and p % BATCH_PAIRS == 1:
                        lay_out_batch(t, p // BATCH_PAIRS - 1, in_last)
                    if p == LAYER1_FROM - 1:
                        lay_out_batch(t, p // BATCH_PAIRS, in_last)
                    if in_last and p > LAYER1_FROM and p % BATCH_PAIRS == 0:
                        lay_out_batch(t, p // BATCH_PAIRS - 1, in_last)
                    if p == LAYER2_FROM and not in_last:
                        lay_out_batch(t, BATCHES // 2, in_last)
                for b in range(BATCHES - 1 if in_last else BATCHES // 2 + 1, BATCHES):
                    lay_out_batch(t, b, in_last)

            act.wait_ge(all_rows_ready, 1)
            act.wait_ge(z_cleared, 1)
            tile(0, True, False)
            with act.Fori(1, n_tiles - 1) as t:
                tile(t, False, False)
            tile(n_tiles - 1, False, True)

        @block.vector
        def _(dve):
            def lay_out_batch(t, b, first, in_last):
                dve.wait_ge(dots_done, t * TILE_PAIRS + (b + 1) * BATCH_PAIRS)
                if not (first and b < 2):
                    dve.wait_ge(z_by_act, t * BATCHES + b - 1)
                columns = dots_ps[b % 4][:, 0:BATCH_GROUPS, :].rearrange("p g (u c) -> p g u c", u=2)
                dve.nop(nofuse=True)
                nc.vector.stream_shuffle(merged[b % 2][:, :, :, :], columns[:, :, :, 0:UPPER],
                                         rotation).then_inc(shuffled, 1)
                dve.wait_ge(shuffled, t * BATCHES + b + 1)
                dve.nop(nofuse=True)
                nc.vector.copy_predicated(merged[b % 2][:, :, :, :], upper_places,
                                          columns[:, :, :, UPPER:]).then_inc(merged_ready, 1)
                dve.wait_ge(merged_ready, t * BATCHES + b + 1)
                lay_out(nc.vector.tensor_copy, b, in_last, range(PER_GROUP // 2)).then_inc(z_by_dve, 1)

            rotation = [(i + UPPER) % FIELDS for i in range(FIELDS)]
            upper_places = upper_sb[:, :].rearrange("p (g u c) -> p g u c", g=1, u=1).to_broadcast(
                [P, BATCH_GROUPS, 2, UPPER])

            def relu1(t):
                dve.wait_ge(l1_done, t + 1)
                nc.vector.tensor_scalar(h1[:, :, :], h1_ps[:, :, :], 0.0, None, ALU.max).then_inc(h1_ready, 1)

            def relu2_chunk(out, ins, n):
                return nc.vector.tensor_scalar(out[:, n, :], ins, b2_sb[:, n:n + 1], 0.0, ALU.add, ALU.max)

            def relu2(t):
                dve.wait_ge(l2_done, t + 1)
                for n in range(n2):
                    last = relu2_chunk(h2, h2_ps[:, n, :], n)
                last.then_inc(h2_ready, 1)

            def store_y(t, sc):
                dve.wait_ge(l3_done, t + 1)
                nc.vector.tensor_copy(y_row[:, sc], h2_ps[0:1, n2, :]).then_inc(y_ready, 1)

            def tile(t, first, in_last):
                if not first:
                    relu2(t - 1)
                for b in range(BATCHES // 2):
                    lay_out_batch(t, b, first, in_last)
                    if b == 0 and not first:
                        store_y(t - 1, bass.ds((t - 1) * TILE, TILE))
                if in_last:
                    for b in range(BATCHES // 2, BATCHES - 2):
                        lay_out_batch(t, b, first, in_last)
                relu1(t)
                for b in range(BATCHES - 2 if in_last else BATCHES // 2, BATCHES):
                    if in_last and b == BATCHES - 1:
                        relu2(t)
                    lay_out_batch(t, b, first, in_last)

            dve.wait_ge(ids_loaded, 16)
            base = ids_sb[:, 0:1]
            nc.vector.tensor_tensor(tile_rows[:, :], ids_sb[:, 1:1 + TILE_GROUPS],
                                    base.to_broadcast([P, TILE_GROUPS]), ALU.add).then_inc(tile_rows_ready, 2)
            nc.vector.tensor_tensor(all_rows[:, :], ids_sb[:, 1:1 + n_groups],
                                    base.to_broadcast([P, n_groups]), ALU.add).then_inc(all_rows_ready, 1)
            nc.vector.memset(z[:, :, 0:HALF], 0.0).then_inc(z_cleared, 1)
            dve.wait_ge(upper_loaded, 16)
            dve.wait_ge(weights_loaded, 16 * weight_dmas)
            tile(0, True, False)
            with dve.Fori(1, n_tiles - 1) as t:
                tile(t, False, False)
            tile(n_tiles - 1, False, True)
            store_y(n_tiles - 1, slice((n_tiles - 1) * TILE, n_tiles * TILE))
            for n in range(n1):
                dve.wait_ge(last_l1_done, n + 1)
                nc.vector.tensor_scalar(h1_last[:, n, :], h1_last_ps[n], 0.0, None, ALU.max).then_inc(last_h1_ready, 1)
            for n in range(n2):
                dve.wait_ge(last_l2_done, n + 1)
                relu2_chunk(h2_last, h2_last_ps[n], n).then_inc(last_h2_ready, 1)
            dve.wait_ge(last_l3_done, 1)
            nc.vector.tensor_copy(y_row[:, samples:], h2_ps[0:1, n2 + 1, 0:HALF]).then_inc(y_ready, 1)


def kernel(**inputs):
    import concourse.bacc as bacc
    from concourse.bass_utils import run_bass_kernel_spmd as run

    tables = [np.asarray(inputs[f"tbl_{f}"]) for f in range(FIELDS)]
    base = np.cumsum([0] + [t.shape[0] for t in tables[:-1]]).astype(np.int32)
    ids = np.asarray(inputs["ids"])
    samples = ids.shape[0]
    groups = samples // PER_GROUP

    w1 = np.asarray(inputs["W_top1"])
    n_pairs = FIELDS * (FIELDS - 1) // 2
    n_dense = w1.shape[0] - n_pairs
    pair_i, pair_j = np.triu_indices(FIELDS, k=1)
    low = pair_j < UPPER
    row, col = np.where(low, pair_j + UPPER, pair_i), np.where(low, pair_i, pair_j - UPPER)
    w1_slots = np.zeros((QUADS, FIELDS, COLS, w1.shape[1]), w1.dtype)
    w1_slots[col // COLS, row, col % COLS] = w1[:n_pairs]
    upper = np.tile(np.arange(FIELDS)[:, None] < UPPER + np.arange(UPPER), (P // FIELDS, 1)).astype(np.int32)

    dense = np.zeros((n_dense + 1, HALF + samples), w1.dtype)
    dense[:n_dense, HALF:] = np.asarray(inputs["dense_ctx"]).T
    dense[n_dense, HALF:] = 1.0

    w2 = np.asarray(inputs["W_top2"])
    arrays = {
        "tables": np.concatenate(tables, axis=0),
        "ids": np.concatenate([
            np.tile(base, PER_GROUP)[:, None],
            ids.reshape(groups, PER_GROUP, FIELDS).transpose(1, 2, 0).reshape(P, groups)], axis=1),
        "w1_slots": w1_slots.reshape(P, -1),
        "w1_dense": np.concatenate([w1[n_pairs:], np.asarray(inputs["b_top1"]).reshape(1, -1)], axis=0),
        "upper": upper,
        "dense": dense,
        "w2": np.ascontiguousarray(
            w2.reshape(-1, P, w2.shape[1]).transpose(1, 0, 2).reshape(P, -1)),
        "b2": np.ascontiguousarray(np.asarray(inputs["b_top2"]).reshape(-1, P).T),
        "w3": np.ascontiguousarray(np.asarray(inputs["W_top3"]).reshape(-1, P).T),
    }
    nc = bacc.Bacc("TRN2", target_bir_lowering=False, num_devices=1)
    aps = {k: nc.dram_tensor(k, v.shape, mybir.dt.from_np(v.dtype), kind="ExternalInput").ap()
           for k, v in arrays.items()}
    y = nc.dram_tensor("y", (1, samples), F32, kind="ExternalOutput").ap()
    build(nc, **aps, y=y)
    r = run(nc, [arrays], core_ids=[0])
    return r.results[0]["y"].reshape(samples, 1)
```
